# Optimizing a Trainium2 kernel written in Bass

```python
import numpy as np
import jax
import jax.numpy as jnp

def _softmax(x, axis=-1):
    return jax.nn.softmax(x, axis=axis)

def _gelu(x):
    return jax.nn.gelu(x, approximate=True)

def _silu(x):
    return jax.nn.silu(x)

def _sigmoid(x):
    return jax.nn.sigmoid(x)

def _layernorm(x, axis=-1, eps=1e-05):
    m = jnp.mean(x, axis=axis, keepdims=True)
    v = jnp.var(x, axis=axis, keepdims=True)
    return (x - m) / jnp.sqrt(v + eps)

def _scatter_add(tgt, idx, src, axis=0):
    return tgt.at[idx].add(src)

def _segment_sum(src, seg, n):
    return jax.ops.segment_sum(src, seg, n)
kernel_name = 'mk_gnn_resnorm_d2_gnn_r32_e44df6'

def setup_inputs(seed: int=0):
    np.random.seed(seed)
    _w = jnp.asarray

    def _rec_inputs():
        import jax
        import jax.numpy as jnp
        _gk = jax.random.key(seed)
        x = -0.000202 + 1 * jax.random.normal(jax.random.fold_in(_gk, 1), (3125, 64), jnp.float32)
        src = jax.random.randint(jax.random.fold_in(_gk, 2), (100000,), 0, 3125, jnp.int32)
        dst = jax.random.randint(jax.random.fold_in(_gk, 3), (100000,), 0, 3125, jnp.int32)
        _o = jnp.argsort(dst, stable=True)
        src = src[_o]
        dst = dst[_o]
        edge_attr_64 = 7.68618e-05 + 1.00005 * jax.random.normal(jax.random.fold_in(_gk, 11), (100000, 64), jnp.float32)
        return (x, src, dst, edge_attr_64)
    x, src, dst, edge_attr_64 = _rec_inputs()

    def _L0_gnn_setup():
        import jax, jax.numpy as jnp
        import numpy as np
        N_NODES = 3125
        N_HEDGES = 625
        N_INC = 18750
        IN_DIM, HID_DIM, OUT_DIM = (64, 128, 64)

        def _glorot(key, shape):
            fan_in, fan_out = (shape[0], shape[1])
            lim = jnp.sqrt(6.0 / (fan_in + fan_out))
            return jax.random.uniform(key, shape, jnp.float32, -lim, lim)

        def _degrees(node_idx, edge_idx):
            ones = jnp.ones((node_idx.shape[0],), jnp.float32)
            D = jax.ops.segment_sum(ones, node_idx, num_segments=N_NODES)
            B = jax.ops.segment_sum(ones, edge_idx, num_segments=N_HEDGES)
            Dinv = jnp.where(D > 0, 1.0 / D, 0.0)
            Binv = jnp.where(B > 0, 1.0 / B, 0.0)
            return (Dinv, Binv)

        def _hconv(x, W, b, node_idx, edge_idx, Dinv, Binv):
            xw = x @ W
            he = jax.ops.segment_sum(xw[node_idx], edge_idx, num_segments=N_HEDGES)
            he = he * Binv[:, None]
            out = jax.ops.segment_sum(he[edge_idx], node_idx, num_segments=N_NODES)
            return out * Dinv[:, None] + b

        def _layernorm(x, g, b, eps=1e-05):
            mu = jnp.mean(x, axis=-1, keepdims=True)
            var = jnp.var(x, axis=-1, keepdims=True)
            return (x - mu) * jax.lax.rsqrt(var + eps) * g + b
        key = jax.random.key(seed)
        ks = jax.random.split(key, 10)
        x = jax.random.normal(ks[0], (N_NODES, IN_DIM), jnp.float32)
        node_idx = jax.random.randint(ks[1], (N_INC,), 0, N_NODES)
        edge_idx = jax.random.randint(ks[2], (N_INC,), 0, N_HEDGES)
        hyperedge_index = jnp.stack([node_idx, edge_idx]).astype(jnp.int64)
        return {'x': x, 'hyperedge_index': hyperedge_index, 'W1': _glorot(ks[3], (IN_DIM, HID_DIM)), 'b1': jnp.zeros((HID_DIM,), jnp.float32), 'g1': jnp.ones((HID_DIM,), jnp.float32), 'beta1': jnp.zeros((HID_DIM,), jnp.float32), 'W2': _glorot(ks[4], (HID_DIM, HID_DIM)), 'b2': jnp.zeros((HID_DIM,), jnp.float32), 'W3': _glorot(ks[5], (HID_DIM, HID_DIM)), 'b3': jnp.zeros((HID_DIM,), jnp.float32), 'W4': _glorot(ks[6], (HID_DIM, HID_DIM)), 'b4': jnp.zeros((HID_DIM,), jnp.float32), 'W5': _glorot(ks[7], (HID_DIM, OUT_DIM)), 'b5': jnp.zeros((OUT_DIM,), jnp.float32)}
    _L0_gnn_all = _L0_gnn_setup()
    _L0_gnn_in = {k: v for k, v in _L0_gnn_all.items() if k in ('W1', 'b1', 'g1', 'beta1', 'W2', 'b2', 'W3', 'b3', 'W4', 'b4', 'W5', 'b5')}
    del _L0_gnn_all

    def _L1_gnn_setup():
        import jax, jax.numpy as jnp
        import numpy as np
        N_NODES = 3125
        N_EDGES = 31250
        D = 64
        key = jax.random.key(seed)
        ks = jax.random.split(key, 12)
        scale = 1.0 / np.sqrt(D)
        inp = {'x': jax.random.normal(ks[0], (N_NODES, D), dtype=jnp.float32), 'edge_index': jax.random.randint(ks[1], (2, N_EDGES), 0, N_NODES, dtype=jnp.int64), 'edge_attr': jax.random.normal(ks[2], (N_EDGES, D), dtype=jnp.float32), 'W1': jax.random.normal(ks[3], (D, D), dtype=jnp.float32) * scale, 'b1': jax.random.normal(ks[4], (D,), dtype=jnp.float32) * scale, 'W2': jax.random.normal(ks[5], (D, D), dtype=jnp.float32) * scale, 'b2': jax.random.normal(ks[6], (D,), dtype=jnp.float32) * scale, 'W3': jax.random.normal(ks[7], (D, D), dtype=jnp.float32) * scale, 'b3': jax.random.normal(ks[8], (D,), dtype=jnp.float32) * scale, 'Wout': jax.random.normal(ks[9], (D, D), dtype=jnp.float32) * scale, 'bout': jax.random.normal(ks[10], (D,), dtype=jnp.float32) * scale}
        return inp
    _L1_gnn_all = _L1_gnn_setup()
    _L1_gnn_in = {k: v for k, v in _L1_gnn_all.items() if k in ('W1', 'b1', 'W2', 'b2', 'W3', 'b3', 'Wout', 'bout')}
    del _L1_gnn_all
    return {'x': x, 'src': src, 'dst': dst, 'edge_attr_64': edge_attr_64, 'L0_gnn_W1': _L0_gnn_in['W1'], 'L0_gnn_b1': _L0_gnn_in['b1'], 'L0_gnn_g1': _L0_gnn_in['g1'], 'L0_gnn_beta1': _L0_gnn_in['beta1'], 'L0_gnn_W2': _L0_gnn_in['W2'], 'L0_gnn_b2': _L0_gnn_in['b2'], 'L0_gnn_W3': _L0_gnn_in['W3'], 'L0_gnn_b3': _L0_gnn_in['b3'], 'L0_gnn_W4': _L0_gnn_in['W4'], 'L0_gnn_b4': _L0_gnn_in['b4'], 'L0_gnn_W5': _L0_gnn_in['W5'], 'L0_gnn_b5': _L0_gnn_in['b5'], 'L1_gnn_W1': _L1_gnn_in['W1'], 'L1_gnn_b1': _L1_gnn_in['b1'], 'L1_gnn_W2': _L1_gnn_in['W2'], 'L1_gnn_b2': _L1_gnn_in['b2'], 'L1_gnn_W3': _L1_gnn_in['W3'], 'L1_gnn_b3': _L1_gnn_in['b3'], 'L1_gnn_Wout': _L1_gnn_in['Wout'], 'L1_gnn_bout': _L1_gnn_in['bout']}

def reference(x, src, dst, edge_attr_64, L0_gnn_W1, L0_gnn_b1, L0_gnn_g1, L0_gnn_beta1, L0_gnn_W2, L0_gnn_b2, L0_gnn_W3, L0_gnn_b3, L0_gnn_W4, L0_gnn_b4, L0_gnn_W5, L0_gnn_b5, L1_gnn_W1, L1_gnn_b1, L1_gnn_W2, L1_gnn_b2, L1_gnn_W3, L1_gnn_b3, L1_gnn_Wout, L1_gnn_bout):
    import jax
    import jax.numpy as jnp

    def _L0_gnn_ref(x, hyperedge_index, W1, b1, g1, beta1, W2, b2, W3, b3, W4, b4, W5, b5):
        import jax, jax.numpy as jnp
        import numpy as np
        N_NODES = 3125
        N_HEDGES = 625
        N_INC = 18750
        IN_DIM, HID_DIM, OUT_DIM = (64, 128, 64)

        def _glorot(key, shape):
            fan_in, fan_out = (shape[0], shape[1])
            lim = jnp.sqrt(6.0 / (fan_in + fan_out))
            return jax.random.uniform(key, shape, jnp.float32, -lim, lim)

        def _degrees(node_idx, edge_idx):
            ones = jnp.ones((node_idx.shape[0],), jnp.float32)
            D = jax.ops.segment_sum(ones, node_idx, num_segments=N_NODES)
            B = jax.ops.segment_sum(ones, edge_idx, num_segments=N_HEDGES)
            Dinv = jnp.where(D > 0, 1.0 / D, 0.0)
            Binv = jnp.where(B > 0, 1.0 / B, 0.0)
            return (Dinv, Binv)

        def _hconv(x, W, b, node_idx, edge_idx, Dinv, Binv):
            xw = x @ W
            he = jax.ops.segment_sum(xw[node_idx], edge_idx, num_segments=N_HEDGES)
            he = he * Binv[:, None]
            out = jax.ops.segment_sum(he[edge_idx], node_idx, num_segments=N_NODES)
            return out * Dinv[:, None] + b

        def _layernorm(x, g, b, eps=1e-05):
            mu = jnp.mean(x, axis=-1, keepdims=True)
            var = jnp.var(x, axis=-1, keepdims=True)
            return (x - mu) * jax.lax.rsqrt(var + eps) * g + b
        node_idx = hyperedge_index[0]
        edge_idx = hyperedge_index[1]
        Dinv, Binv = _degrees(node_idx, edge_idx)
        h = _hconv(x, W1, b1, node_idx, edge_idx, Dinv, Binv)
        h = jax.nn.relu(_layernorm(h, g1, beta1))
        h = jax.nn.relu(_hconv(h, W2, b2, node_idx, edge_idx, Dinv, Binv))
        h = jax.nn.relu(_hconv(h, W3, b3, node_idx, edge_idx, Dinv, Binv))
        h = jax.nn.relu(_hconv(h, W4, b4, node_idx, edge_idx, Dinv, Binv))
        z = _hconv(h, W5, b5, node_idx, edge_idx, Dinv, Binv)
        return z

    def _L1_gnn_ref(x, edge_index, edge_attr, W1, b1, W2, b2, W3, b3, Wout, bout):
        import jax, jax.numpy as jnp
        import numpy as np
        N_NODES = 3125
        N_EDGES = 31250
        D = 64
        src = edge_index[0]
        dst = edge_index[1]
        n = x.shape[0]
        counts = jax.ops.segment_sum(jnp.ones((edge_index.shape[1],), dtype=x.dtype), dst, num_segments=n)
        denom = jnp.maximum(counts, 1.0)[:, None]
        for W, b in ((W1, b1), (W2, b2), (W3, b3)):
            gate = edge_attr @ W.T + b
            msg = x[src] * gate
            agg = jax.ops.segment_sum(msg, dst, num_segments=n)
            x = jax.nn.relu(agg / denom)
        return x @ Wout.T + bout
    edge_index = jnp.stack([src, dst])
    x = _layernorm(x + _L0_gnn_ref(x, edge_index, L0_gnn_W1, L0_gnn_b1, L0_gnn_g1, L0_gnn_beta1, L0_gnn_W2, L0_gnn_b2, L0_gnn_W3, L0_gnn_b3, L0_gnn_W4, L0_gnn_b4, L0_gnn_W5, L0_gnn_b5), axis=-1)
    x = _layernorm(x + _L1_gnn_ref(x, edge_index, edge_attr_64, L1_gnn_W1, L1_gnn_b1, L1_gnn_W2, L1_gnn_b2, L1_gnn_W3, L1_gnn_b3, L1_gnn_Wout, L1_gnn_bout), axis=-1)
    return x

_drawn_inputs = setup_inputs


def setup_inputs(seed=0):
    import zlib

    import numpy as np

    out = dict(_drawn_inputs(seed))
    spreads = {'L0_gnn_b1': (0.0, 0.1),
     'L0_gnn_g1': (1.0, 0.2),
     'L0_gnn_beta1': (0.0, 0.282),
     'L0_gnn_b2': (0.0, 0.1),
     'L0_gnn_b3': (0.0, 0.1),
     'L0_gnn_b4': (0.0, 0.1),
     'L0_gnn_b5': (0.0, 0.1)}
    factors = {'edge_attr_64': 8.0,
     'L1_gnn_W1': 8.0,
     'L1_gnn_b1': 8.0,
     'L1_gnn_W2': 8.0,
     'L1_gnn_b2': 8.0,
     'L1_gnn_W3': 8.0,
     'L1_gnn_b3': 8.0,
     'L1_gnn_Wout': 8.0}
    for name, (base, spread) in spreads.items():
        noise = np.random.default_rng([zlib.crc32(name.encode()), seed]).standard_normal(out[name].shape)
        drawn = base * np.exp(spread * noise) if base else spread * noise
        out[name] = jnp.asarray(drawn.astype(out[name].dtype))
    for name, factor in factors.items():
        out[name] = (out[name] * factor).astype(out[name].dtype)
    return out
```

```python
from contextlib import ExitStack

import concourse.bass as bass
from concourse import mybir

P = 128
N_NODES, N_HEDGES, N_EDGES = 3125, 625, 100000
D, HID = 64, 128
C = -(-N_NODES // P)
NODES_PAD = C * P
KH = -(-N_HEDGES // P)
H_PAD = KH * P
T = 8
GROUP = T * P
G = -(-N_EDGES // GROUP)
EDGES_PAD = G * GROUP
HW = 16
NHW = H_PAD // HW
KEYS = C * HW
LAST_H = N_HEDGES - 1
CONVS, LAYERS = 5, 3
EPS = 1e-5
ROW_B, ROW_G1, ROW_BETA1, ROW_L1B, ROW_BOUT = 0, 640, 768, 896, 1088
ROWS = 1152
W_L0, W_L1, W_OUT = 0, 640, 832
WEIGHTS = 896


def gnn_program(nc, src_in, dst_in, edge_in, x_in, w_in, rows_in, out_dram):
    f32, i32 = mybir.dt.float32, mybir.dt.int32
    bf16, f16 = mybir.dt.bfloat16, mybir.dt.float16
    ALU, ACT, AX = mybir.AluOpType, mybir.ActivationFunctionType, mybir.AxisListType
    X = AX.X

    ctx = ExitStack()
    with ctx:
        def sb(name, shape, dt=f32):
            return ctx.enter_context(nc.sbuf_tensor(name, shape, dt))

        def sem(name):
            return ctx.enter_context(nc.semaphore(name))

        table = nc.dram_tensor("x_table", [NODES_PAD, D], f32).ap()

        at_all = sb("at_all", [P, C * H_PAD])
        a2_all = sb("a2_all", [P, KH * NODES_PAD])
        AT = at_all[:, :].rearrange("p (c h) -> p c h", c=C)
        A2 = a2_all[:, :].rearrange("p (k n) -> p k n", k=KH)
        src_i = sb("src_i", [P, G * T], i32)
        dst_i = sb("dst_i", [P, G * T], i32)
        dst_f = sb("dst_f", [P, G * T])
        weights = sb("weights", [P, WEIGHTS])
        rows = sb("rows", [P, ROWS])
        x0 = sb("x0", [P, C, D])
        H = sb("H", [P, C, HID])
        x1 = sb("x1", [P, C, D])
        PT = sb("PT", [P, H_PAD])
        HE = sb("HE", [P, KH, HID])
        ident = sb("ident", [P, P])
        upper = sb("upper", [P, P])
        iota_f = sb("iota_f", [P, P])
        iota_h = sb("iota_h", [P, P], f16)
        iota_key = sb("iota_key", [P, KEYS], f16)
        iota_w = sb("iota_w", [P, NHW])
        pcol = sb("pcol", [P, 1])
        gidx = sb("gidx", [1, G])
        mm = sb("mm", [P, 2, G])
        cols = sb("cols", [P, 8])
        cols_i = sb("cols_i", [P, 4], i32)
        rowt = sb("rowt", [1, 7 * G])
        tab_f = sb("tab_f", [1, 12 * G])
        tab_i = sb("tab_i", [1, 12 * G], i32)
        ng_f = sb("ng_f", [1, 2])
        ng_i = sb("ng_i", [1, 1], i32)
        deg = sb("deg", [P, C])
        deg_inv = sb("deg_inv", [P, C])
        b_part = sb("b_part", [P, KH, 7])
        b_inv = sb("b_inv", [P, KH])
        col_new = sb("col_new", [P, C])
        col_old = sb("col_old", [P, C])
        small = sb("small", [P, 4, C])
        edge_t = [sb(f"edge_t{b}", [P, 4 * P]) for b in range(2)]

        def early(lo, n, dt=f32):
            v = a2_all[:, lo:lo + n]
            return v if dt == f32 else v.bitcast(dt)
        GT = G * T
        src_lo, src_hi = early(0, GT), early(GT, GT)
        key, dst_hi = early(2 * GT, GT), early(3 * GT, GT)
        tmp_i = early(4 * GT, GT, i32)
        at = 5 * GT
        oh_r = [early(at + 512 * b, 512, bf16).rearrange("p (t j) -> p t j", t=T) for b in range(2)]
        at += 1024
        oh_c = [early(at + 100 * b, 100, bf16).rearrange("p (t j) -> p t j", t=T) for b in range(2)]
        at += 200
        oh_k = early(at, T * KEYS // 2, bf16).rearrange("p (t j) -> p t j", t=T)
        at += T * KEYS // 2
        stage = early(at, T)
        key2 = early(at + T, T)
        def late(lo, n):
            return at_all[:, lo:lo + n]
        xg = [late(512 * b, 512).rearrange("p (t f) -> p t f", t=T) for b in range(2)]
        gate = late(1024, 512).rearrange("p (t f) -> p t f", t=T)
        msg = [late(1536 + 520 * b, 520).rearrange("p (t f) -> p t f", t=T) for b in range(2)]
        oh = late(2576, 1024).rearrange("p (t j) -> p t j", t=T)
        agg = late(3600, C * (D + 1)).rearrange("p (c f) -> p c f", c=C)
        xn = late(5300, C * D).rearrange("p (c f) -> p c f", c=C)
        iota_n = late(7000, NODES_PAD)
        xT = late(10200, P)
        x3 = late(10400, C * D).rearrange("p (c f) -> p c f", c=C)
        w_cur = late(12100, D)
        b_cur = late(12200, D)
        sq = a2_all[:, 0:C * HID].rearrange("p (c f) -> p c f", c=C)
        idx = [sb(f"idx{b}", [P, T], i32) for b in range(2)]

        bank = ctx.enter_context(nc.psum_tensor("bank", [P, 8, 512], f32))

        s_edges = sem("edges_loaded")
        s_x = sem("x_loaded")
        s_w = sem("weights_loaded")
        pool_consts = sem("pool_consts")
        minmax_ready = sem("minmax_ready")
        minmax_turned = sem("minmax_turned")
        cols_ready = sem("cols_ready")
        rows_ready = sem("rows_ready")
        tables_ready = sem("tables_ready")
        hist_oh = sem("hist_onehots_ready")
        hist_free = sem("hist_onehots_free")
        cnt_oh = sem("count_onehots_ready")
        cnt_done = sem("count_visit_done")
        cnt_added = sem("count_visit_added")
        at_ready = sem("at_ready")
        turned = sem("count_blocks_turned")
        turned_kept = sem("count_blocks_kept")
        col_swapped = sem("last_column_swapped")
        h_ready = sem("h_ready")
        p1_done = sem("stage1_done")
        pt_ready = sem("stage1_kept")
        he_done = sem("he_product_done")
        he_ready = sem("he_ready")
        out_done = sem("stage2_chunks_done")
        out_free = sem("stage2_bank_free")
        var_ready = sem("variance_ready")
        std_ready = sem("std_ready")
        xn_ready = sem("table_rows_ready")
        table_written = sem("table_written")
        iota_ready = sem("node_iota_ready")
        late_free = sem("convolutions_done")
        edge_ready = [sem(f"edge_ready{b}") for b in range(2)]
        idx_ready = sem("idx_ready")
        xg_ready = [sem(f"gathered{b}") for b in range(2)]
        xg_free = sem("gather_buffer_free")
        gathers_begun = sem("gathers_begun")
        sums_begun = sem("sums_begun")
        w_cur_ready = sem("layer_weights_ready")
        gates_done = sem("gates_done")
        gates_read = sem("gate_bank_free")
        msg_ready = sem("messages_ready")
        oh_ready = sem("node_onehots_ready")
        vis_done = sem("visit_done")
        agg_added = sem("visit_added")
        x3_ready = sem("x3_ready")
        xT_psum = sem("xT_in_psum")
        xT_kept = sem("xT_kept")
        fin_done = sem("final_product_done")
        fin_read = sem("final_bank_free")
        out_ready = sem("out_rows_ready")
        stored = sem("out_stored")

        block = ctx.enter_context(nc.Block())

        def entry(kind, row):
            return (kind * 4 + row) * G

        def load_visits(eng, row, g):
            at = G * row + g if isinstance(row, int) else row * G + g
            vs = eng.value_load(tab_i[0:1, bass.ds(at, 1)], min_val=0, max_val=4 * G * NHW)
            ve = eng.value_load(tab_i[0:1, bass.ds(at + 4 * G, 1)], min_val=1, max_val=4 * G * NHW)
            return at, vs, ve

        def load_offset(eng, at, v, top):
            off = eng.value_load(tab_i[0:1, bass.ds(at + 8 * G, 1)], min_val=-4 * G * NHW, max_val=NHW)
            def window(v):
                return nc.s_assert_within(v + off, 0, top,
                                          skip_runtime_bounds_check_because="windows come from clamped minima and maxima")
            return window

        @block.sync
        def _(sp):
            sp.dma_start(src_i[:, :], src_in).then_inc(s_edges, 16)
            sp.dma_start(dst_i[:, :], dst_in).then_inc(s_edges, 16)
            sp.dma_start(x0[:, :, :], x_in).then_inc(s_x, 16)
            sp.dma_start(weights[:, :], w_in).then_inc(s_w, 16)
            sp.dma_start(rows[:, :], rows_in).then_inc(s_w, 16)
            table_v = table.rearrange("(c p) f -> p c f", p=P)
            with sp.Fori(0, LAYERS) as layer:
                sp.wait_ge(xn_ready, layer + 1)
                sp.dma_start(table_v, xn).then_inc(table_written, 16)
                with sp.Fori(0, G // 2) as i:
                    for b in range(2):
                        sp.wait_ge(gates_read, layer * G + 2 * i + b + 1)
                        sp.dma_start(edge_t[b][:, :], edge_in[bass.ds(2 * i + b, 1), :, :].rearrange("g p n -> p (g n)"))\
                          .then_inc(edge_ready[b], 16)
            sp.wait_ge(out_ready, 1)
            whole = (C - 1) * P
            sp.dma_start(out_dram[0:whole, :].rearrange("(c p) f -> p c f", p=P), xn[:, 0:C - 1, :]).then_inc(stored, 16)
            sp.dma_start(out_dram[whole:N_NODES, :], xn[0:N_NODES - whole, C - 1, :]).then_inc(stored, 16)
            sp.wait_ge(stored, 32)

        @block.gpsimd
        def _(pool):
            small_ok = dict(allow_small_or_imprecise_dtypes=True)
            pool.iota(iota_f[:, :], [[1, P]], base=0, channel_multiplier=0, **small_ok).then_inc(pool_consts, 1)
            pool.iota(iota_key[:, :], [[1, KEYS]], base=0, channel_multiplier=0, **small_ok).then_inc(pool_consts, 1)
            pool.iota(iota_w[:, :], [[1, NHW]], base=0, channel_multiplier=0, **small_ok).then_inc(pool_consts, 1)
            pool.iota(pcol[:, :], [[0, 1]], base=0, channel_multiplier=1, **small_ok).then_inc(pool_consts, 1)
            pool.iota(gidx[:, :], [[1, G]], base=1, channel_multiplier=0, **small_ok).then_inc(pool_consts, 1)
            pool.wait_ge(late_free, 1)
            pool.iota(iota_n, [[1, NODES_PAD]], base=0, channel_multiplier=0, **small_ok).then_inc(iota_ready, 1)
            with pool.Fori(0, LAYERS) as layer:
                pool.wait_ge(table_written, (layer + 1) * 16)
                pool.sem_inc(gathers_begun, 1)
                with pool.Fori(0, G // 2) as i:
                    for b in range(2):
                        q = layer * G + 2 * i + b
                        pool.wait_ge(idx_ready, q + 1)
                        pool.wait_ge(xg_free, q + 1)
                        pool.sem_inc(gathers_begun, 1)
                        for t in range(T):
                            pool.indirect_dma_start(
                                xg[b][:, t, :], None, table,
                                bass.IndirectOffsetOnAxis(ap=idx[b][:, t:t + 1], axis=0)).then_inc(xg_ready[b], 16)

        @block.scalar
        def _(act):
            act.wait_ge(at_ready, 1)
            n = 0
            for k in list(range(KH)) + [KH - 1]:
                for j in range(7):
                    w = min(4, C - 4 * j) * P
                    act.wait_ge(turned, n + 1)
                    kept = A2[:, k, 4 * j * P:4 * j * P + w]
                    if n < KH * 7:
                        nc.scalar.activation(kept, bank[:, 4 + n % 4, 0:w], ACT.Copy,
                                             accum_out=b_part[:, k, j:j + 1]).then_inc(turned_kept, 1)
                    else:
                        nc.scalar.activation(kept, bank[:, 4 + n % 4, 0:w], ACT.Copy).then_inc(turned_kept, 1)
                    n += 1
            for norm in range(2):
                act.wait_ge(var_ready, norm + 1)
                nc.scalar.activation(small[:, 2, :], small[:, 1, :], ACT.Sqrt).then_inc(std_ready, 1)
            act.wait_ge(late_free, 1)
            with act.Fori(0, LAYERS) as layer:
                act.wait_ge(gates_read, layer * G + 2)
                nc.scalar.copy(w_cur, weights[:, bass.ds(layer * D + W_L1, D)]).then_inc(w_cur_ready, 1)
                nc.scalar.copy(b_cur, rows[:, bass.ds(layer * D + ROW_L1B, D)]).then_inc(w_cur_ready, 1)
                with act.Fori(0, G // 2) as i:
                    for b in range(2):
                        act.wait_ge(xg_free, layer * G + 2 * i + b + 1)
                        nc.scalar.copy(idx[b][:, :], src_i[:, bass.ds((2 * i + b) * T, T)]).then_inc(idx_ready, 1)
            act.wait_ge(var_ready, 3)
            nc.scalar.activation(small[:, 2, :], small[:, 1, :], ACT.Sqrt).then_inc(std_ready, 1)

        @block.tensor
        def _(pe):
            pe.sem_inc(hist_free, 2)
            pe.wait_ge(minmax_ready, 1)
            nc.tensor.transpose(bank[0:G, 2, 0:P], mm[:, 0, :], ident[:, :])
            nc.tensor.transpose(bank[0:G, 2, P:2 * P], mm[:, 1, :], ident[:, :]).then_inc(minmax_turned, 1)
            pe.wait_ge(cols_ready, 1)
            for n, (col, by) in enumerate([(0, ident), (1, ident), (1, upper)]):
                nc.tensor.matmul(bank[0:1, 2, n * G:(n + 1) * G], cols[0:G, col:col + 1], by[0:G, 0:G], start=True, stop=True)
            for n, (col, by) in enumerate([(2, ident), (3, ident), (3, upper), (4, ident)]):
                last = nc.tensor.matmul(bank[0:1, 3, n * G:(n + 1) * G], cols[0:G, col:col + 1], by[0:G, 0:G], start=True, stop=True)
            last.then_inc(rows_ready, 1)
            with pe.Fori(0, G // 2) as i:
                for b in range(2):
                    pe.wait_ge(hist_oh, 2 * i + b + 1)
                    for t in range(T):
                        last = nc.tensor.matmul(bank[:, 0, 0:C], oh_r[b][:, t, :], oh_c[b][:, t, :],
                                                start=False, stop=False, skip_group_check=True)
                    last.then_inc(hist_free, 1)
            pe.wait_ge(tables_ready, 1)
            n_groups = pe.value_load(ng_i[0:1, 0:1], min_val=1, max_val=G)
            with pe.Fori(0, n_groups) as g:
                _, vs, ve = load_visits(pe, 3, g)
                with pe.Fori(vs, ve) as v:
                    pe.wait_ge(cnt_oh, v + 1)
                    pe.wait_ge(cnt_added, v + 1)
                    for t in range(T):
                        last = nc.tensor.matmul(bank[:, 1, 0:KEYS], oh_r[0][:, t, :], oh_k[:, t, :],
                                                start=(t == 0), stop=(t == T - 1))
                    last.then_inc(cnt_done, 1)
            pe.wait_ge(at_ready, 1)
            n = 0
            for r, k in enumerate(list(range(KH)) + [KH - 1]):
                if r == KH:
                    pe.wait_ge(col_swapped, 1)
                for j in range(7):
                    if n >= 4:
                        pe.wait_ge(turned_kept, n - 3)
                    for c in range(4 * j, min(4 * j + 4, C)):
                        last = nc.tensor.transpose(bank[:, 4 + n % 4, (c - 4 * j) * P:(c - 4 * j + 1) * P],
                                                   AT[:, c, k * P:(k + 1) * P], ident[:, :])
                    last.then_inc(turned, 1)
                    n += 1

            def conv(n, fin, fout):
                pe.wait_ge(h_ready, n + 1)
                for c in range(C):
                    for half in range(2):
                        last = nc.tensor.matmul(bank[0:fin, half, 0:H_PAD // 2], H[:, c, 0:fin],
                                                AT[:, c, half * (H_PAD // 2):(half + 1) * (H_PAD // 2)],
                                                start=(c == 0), stop=(c == C - 1))
                last.then_inc(p1_done, 1)
                pe.wait_ge(pt_ready, n + 1)
                for k in range(KH):
                    last = nc.tensor.matmul(bank[:, 2 + k // 4, (k % 4) * P:(k % 4) * P + fout], PT[0:fin, k * P:(k + 1) * P],
                                            weights[0:fin, bass.ds(n * HID + W_L0, fout)], start=True, stop=True)
                last.then_inc(he_done, 1)
                pe.wait_ge(he_ready, n + 1)
                for j in range(7):
                    pe.wait_ge(out_free, n * 7 + j + 1)
                    for c in range(4 * j, min(4 * j + 4, C)):
                        for k in range(KH):
                            last = nc.tensor.matmul(bank[:, 4 + j % 2, (c - 4 * j) * P:(c - 4 * j) * P + fout],
                                                    A2[:, k, c * P:(c + 1) * P], HE[:, k, 0:fout],
                                                    start=(k == 0), stop=(k == KH - 1))
                    last.then_inc(out_done, 1)

            pe.wait_ge(s_w, 32)
            pe.wait_ge(turned_kept, (KH + 1) * 7)
            conv(0, D, HID)
            with pe.Fori(1, CONVS - 1) as n:
                conv(n, HID, HID)
            conv(CONVS - 1, HID, D)

            def gates(layer, i, b):
                q = layer * G + 2 * i + b
                pe.wait_ge(edge_ready[b], (layer * (G // 2) + i + 1) * 16)
                pe.wait_ge(gates_read, q + 1)
                for t in range(T // 2):
                    for half in range(2):
                        p = half * D
                        last = nc.tensor.matmul(bank[:, 2 * b + half, t * D:(t + 1) * D], edge_t[b][p:p + D, t * P:(t + 1) * P],
                                                w_cur[p:p + D, :], start=True, stop=True)
                last.then_inc(gates_done, 1)

            def visits(layer, i, b):
                g = 2 * i + b
                pe.wait_ge(msg_ready, layer * G + g + 1)
                _, vs, ve = load_visits(pe, layer, g)
                with pe.Fori(vs, ve) as v:
                    pe.wait_ge(oh_ready, v + 1)
                    pe.wait_ge(agg_added, v + 1)
                    for t in range(T):
                        last = nc.tensor.matmul(bank[:, 4, 0:D + 1], oh[:, t, :], msg[b][:, t, :],
                                                start=(t == 0), stop=(t == T - 1))
                    last.then_inc(vis_done, 1)

            with pe.Fori(0, LAYERS) as layer:
                pe.wait_ge(w_cur_ready, (layer + 1) * 2)
                gates(layer, 0, 0)
                with pe.Fori(0, G // 2 - 1) as i:
                    gates(layer, i, 1)
                    visits(layer, i, 0)
                    gates(layer, i + 1, 0)
                    visits(layer, i, 1)
                gates(layer, G // 2 - 1, 1)
                visits(layer, G // 2 - 1, 0)
                visits(layer, G // 2 - 1, 1)

            pe.wait_ge(x3_ready, 1)
            for c in range(C):
                nc.tensor.transpose(bank[0:D, 5, 0:P], x3[:, c, :], ident[:, :]).then_inc(xT_psum, 1)
                pe.wait_ge(xT_kept, c + 1)
                if c >= 2:
                    pe.wait_ge(fin_read, c - 1)
                nc.tensor.matmul(bank[:, 6 + c % 2, 0:D], xT[0:D, :], weights[0:D, W_OUT:W_OUT + D],
                                 start=True, stop=True).then_inc(fin_done, 1)

        @block.vector
        def _(dve):
            v_ = nc.vector
            dve.sem_inc(gates_read, 2)
            dve.sem_inc(xg_free, 2)
            dve.sem_inc(cnt_added, 1)
            dve.sem_inc(agg_added, 1)
            dve.wait_ge(pool_consts, 5)
            v_.tensor_scalar(ident[:, :], iota_f[:, :], pcol[:, :], None, ALU.is_equal)
            v_.tensor_scalar(upper[:, :], iota_f[:, :], pcol[:, :], None, ALU.is_ge)
            v_.tensor_copy(iota_h[:, :], iota_f[:, :])
            v_.memset(bank[:, 0, 0:C], 0.0)
            v_.memset(at_all[:, :], 0.0)
            dve.wait_ge(s_edges, 32)
            v_.tensor_copy(dst_f[:, :], dst_i[:, :])
            v_.tensor_scalar(tmp_i, src_i[:, :], 7, None, ALU.logical_shift_right)
            dve.drain()
            for end in range(2):
                op = (ALU.min, ALU.max)[end]
                v_.tensor_reduce(mm[:, end, :], dst_f[:, :].rearrange("p (g t) -> p g t", t=T), X, op)
            v_.tensor_copy(src_hi, tmp_i)
            dve.drain().then_inc(minmax_ready, 1)
            v_.tensor_scalar(tmp_i, src_i[:, :], P - 1, None, ALU.bitwise_and)
            dve.drain()
            v_.tensor_copy(src_lo, tmp_i)
            dve.drain()
            v_.tensor_scalar(tmp_i, dst_i[:, :], HW - 1, None, ALU.bitwise_and)
            dve.drain()
            v_.scalar_tensor_tensor(key, src_hi, float(HW), tmp_i, ALU.mult, ALU.add)
            dve.drain()
            v_.tensor_scalar(tmp_i, dst_i[:, :], 4, None, ALU.logical_shift_right)
            dve.drain()
            v_.tensor_copy(dst_hi, tmp_i)
            dve.wait_ge(minmax_turned, 1)
            v_.tensor_reduce(cols[0:G, 4:5], bank[0:G, 2, 0:P], X, ALU.min)
            v_.tensor_reduce(cols[0:G, 5:6], bank[0:G, 2, P:2 * P], X, ALU.max)
            dve.drain()
            v_.tensor_copy(cols_i[0:G, 0:2], cols[0:G, 4:6])
            dve.drain()
            v_.tensor_scalar(cols_i[0:G, 2:4], cols_i[0:G, 0:2], 7, None, ALU.logical_shift_right)
            dve.drain()
            v_.tensor_copy(cols[0:G, 0:2], cols_i[0:G, 2:4])
            dve.drain()
            v_.tensor_scalar(cols_i[0:G, 2:4], cols_i[0:G, 0:2], 4, None, ALU.logical_shift_right)
            dve.drain()
            v_.tensor_scalar(cols[0:G, 2:4], cols_i[0:G, 2:4], float(NHW - 1), None, ALU.min)
            dve.drain()
            for at in (0, 2):
                v_.scalar_tensor_tensor(cols[0:G, at + 1:at + 2], cols[0:G, at + 1:at + 2], 1.0, cols[0:G, at:at + 1],
                                        ALU.add, ALU.subtract)
            dve.drain().then_inc(cols_ready, 1)
            dve.wait_ge(rows_ready, 1)
            v_.tensor_copy(rowt[:, 0:3 * G], bank[0:1, 2, 0:3 * G])
            v_.tensor_copy(rowt[:, 3 * G:7 * G], bank[0:1, 3, 0:4 * G])
            dve.drain()
            for row, at in ((0, 0), (3, 3 * G)):
                lo, nv, ve = (rowt[:, at + n * G:at + (n + 1) * G] for n in range(3))
                first, end, off = (tab_f[:, entry(n, row):entry(n, row) + G] for n in range(3))
                v_.tensor_copy(end, ve)
                v_.tensor_sub(first, ve, nv)
                dve.drain()
                v_.tensor_sub(off, lo, first)
            for layer in range(1, LAYERS):
                total = rowt[:, 3 * G - 1:3 * G]
                dve.drain()
                for kind, op in ((0, ALU.add), (1, ALU.add), (2, ALU.subtract)):
                    a, z = entry(kind, layer - 1), entry(kind, layer)
                    v_.tensor_scalar(tab_f[:, z:z + G], tab_f[:, a:a + G], total, None, op)
            least = rowt[:, 6 * G:7 * G]
            v_.scalar_tensor_tensor(mm[0:1, 0, :], least, float(N_HEDGES), gidx[:, :], ALU.is_lt, ALU.mult)
            dve.drain()
            v_.tensor_reduce(ng_f[:, 0:1], mm[0:1, 0, :], X, ALU.max)
            dve.drain()
            v_.tensor_scalar(ng_i[:, :], ng_f[:, 0:1], 1.0, None, ALU.max)
            v_.tensor_copy(tab_i[:, :], tab_f[:, :])
            dve.drain().then_inc(tables_ready, 1)

            with dve.Fori(0, G // 2) as i:
                for b in range(2):
                    g8 = (2 * i + b) * T
                    dve.wait_ge(hist_free, 2 * i + b + 1)
                    v_.tensor_copy(stage, src_lo[:, bass.ds(g8, T)])
                    v_.tensor_tensor(oh_c[b], src_hi[:, bass.ds(g8, T)].unsqueeze(2).broadcast_to((P, T, C)),
                                     iota_f[:, 0:C].unsqueeze(1).broadcast_to((P, T, C)), ALU.is_equal)
                    dve.drain()
                    for t in range(T):
                        v_.tensor_scalar(oh_r[b][:, t, :], iota_h[:, :], stage[:, t:t + 1], None, ALU.is_equal)
                    dve.drain().then_inc(hist_oh, 1)
            dve.wait_ge(hist_free, G + 2)
            v_.tensor_copy(deg[:, :], bank[:, 0, 0:C])

            n_groups = dve.value_load(ng_i[0:1, 0:1], min_val=1, max_val=G)
            with dve.Fori(0, n_groups) as g:
                v_.tensor_copy(stage, src_lo[:, bass.ds(g * T, T)])
                dve.drain()
                for t in range(T):
                    v_.tensor_scalar(oh_r[0][:, t, :], iota_h[:, :], stage[:, t:t + 1], None, ALU.is_equal)
                at, vs, ve = load_visits(dve, 3, g)
                window = load_offset(dve, at, None, NHW - 1)
                with dve.Fori(vs, ve) as v:
                    w = window(v)
                    v_.tensor_scalar(key2, dst_hi[:, bass.ds(g * T, T)], iota_w[:, bass.ds(w, 1)], 4096.0,
                                     ALU.not_equal, ALU.mult)
                    dve.drain()
                    v_.tensor_add(key2, key2, key[:, bass.ds(g * T, T)])
                    dve.drain()
                    for t in range(T):
                        v_.tensor_scalar(oh_k[:, t, :], iota_key[:, :], key2[:, t:t + 1], None, ALU.is_equal)
                    dve.drain().then_inc(cnt_oh, 1)
                    dve.wait_ge(cnt_done, v + 1)
                    part = AT[:, :, bass.ds(w * HW, HW)]
                    v_.tensor_tensor(part, part, bank[:, 1, 0:KEYS].rearrange("p (c h) -> p c h", c=C), ALU.add)\
                      .then_inc(cnt_added, 1)
                dve.drain()
            v_.memset(AT[:, :, N_HEDGES:H_PAD], 0.0)
            dve.drain().then_inc(at_ready, 1)
            v_.tensor_reduce(col_new[:, :], AT[:, :, 0:LAST_H], X, ALU.add)
            v_.tensor_copy(col_old[:, :], AT[:, :, LAST_H])
            dve.drain()
            v_.tensor_sub(col_new[:, :], deg[:, :], col_new[:, :])
            v_.tensor_scalar(small[:, 0, :], deg[:, :], 1.0, None, ALU.max)
            v_.tensor_scalar(small[:, 1, :], deg[:, :], 0.0, None, ALU.is_gt)
            dve.drain()
            v_.reciprocal(deg_inv[:, :], small[:, 0, :])
            dve.drain()
            v_.tensor_mul(deg_inv[:, :], deg_inv[:, :], small[:, 1, :])
            dve.wait_ge(turned, KH * 7)
            v_.tensor_copy(AT[:, :, LAST_H], col_new[:, :])
            dve.drain().then_inc(col_swapped, 1)
            dve.wait_ge(turned_kept, KH * 7)
            v_.tensor_reduce(b_inv[:, :], b_part[:, :, :], X, ALU.add)
            dve.drain()
            v_.tensor_scalar(small[:, 0, 0:KH], b_inv[:, :], 1.0, None, ALU.max)
            v_.tensor_scalar(small[:, 1, 0:KH], b_inv[:, :], 0.0, None, ALU.is_gt)
            dve.drain()
            v_.reciprocal(b_inv[:, :], small[:, 0, 0:KH])
            dve.drain()
            v_.tensor_mul(b_inv[:, :], b_inv[:, :], small[:, 1, 0:KH])
            dve.wait_ge(turned, (KH + 1) * 7)
            v_.tensor_copy(AT[:, :, LAST_H], col_old[:, :])
            dve.wait_ge(s_x, 16)
            v_.tensor_copy(H[:, :, 0:D], x0[:, :, :])
            dve.sem_inc(out_free, 2)
            dve.drain().then_inc(h_ready, 1)
            dve.wait_ge(s_w, 32)

            def conv(n, fin, fout):
                dve.wait_ge(p1_done, n + 1)
                v_.tensor_copy(PT[0:fin, :].rearrange("p (a h) -> p a h", a=2), bank[0:fin, 0:2, 0:H_PAD // 2])\
                  .then_inc(pt_ready, 1)
                dve.wait_ge(he_done, n + 1)
                for k in range(KH):
                    v_.tensor_scalar(HE[:, k, 0:fout], bank[:, 2 + k // 4, (k % 4) * P:(k % 4) * P + fout],
                                     b_inv[:, k:k + 1], None, ALU.mult)
                dve.drain().then_inc(he_ready, 1)
                for j in range(7):
                    dve.wait_ge(out_done, n * 7 + j + 1)
                    for c in range(4 * j, min(4 * j + 4, C)):
                        last = v_.scalar_tensor_tensor(
                            H[:, c, 0:fout], bank[:, 4 + j % 2, (c - 4 * j) * P:(c - 4 * j) * P + fout],
                            deg_inv[:, c:c + 1], rows[:, bass.ds(n * HID + ROW_B, fout)], ALU.mult, ALU.add)
                    last.then_inc(out_free, 1)
                dve.drain()

            def over(ap, width):
                return ap.unsqueeze(2).broadcast_to((P, C, width))

            def along(ap, width):
                return ap.unsqueeze(1).broadcast_to((P, C, width))

            def normalise(x, width, norm):
                v_.tensor_reduce(small[:, 0, :], x, X, ALU.add)
                dve.drain()
                v_.tensor_scalar(small[:, 0, :], small[:, 0, :], 1.0 / width, None, ALU.mult)
                dve.drain()
                v_.tensor_tensor(x, x, over(small[:, 0, :], width), ALU.subtract)
                dve.drain()
                v_.tensor_mul(sq[:, :, 0:width], x, x)
                dve.drain()
                v_.tensor_reduce(small[:, 1, :], sq[:, :, 0:width], X, ALU.add)
                dve.drain()
                v_.tensor_scalar(small[:, 1, :], small[:, 1, :], 1.0 / width, EPS, ALU.mult, ALU.add).then_inc(var_ready, 1)
                dve.wait_ge(std_ready, norm + 1)
                v_.reciprocal(small[:, 3, :], small[:, 2, :])
                dve.drain()
                v_.tensor_tensor(x, x, over(small[:, 3, :], width), ALU.mult)
                dve.drain()

            conv(0, D, HID)
            hid_norm = HID
            v_.tensor_reduce(small[:, 0, :], H[:, :, :], X, ALU.add)
            dve.drain()
            v_.tensor_scalar(small[:, 0, :], small[:, 0, :], 1.0 / hid_norm, None, ALU.mult)
            dve.drain()
            v_.tensor_tensor(H[:, :, :], H[:, :, :], over(small[:, 0, :], HID), ALU.subtract)
            dve.drain()
            for half in range(2):
                part = H[:, :, half * D:(half + 1) * D]
                v_.tensor_mul(x1[:, :, :], part, part)
                dve.drain()
                v_.tensor_reduce(small[:, 1 + 2 * half, :], x1[:, :, :], X, ALU.add)
                dve.drain()
            v_.tensor_add(small[:, 1, :], small[:, 1, :], small[:, 3, :])
            dve.drain()
            v_.tensor_scalar(small[:, 1, :], small[:, 1, :], 1.0 / hid_norm, EPS, ALU.mult, ALU.add).then_inc(var_ready, 1)
            dve.wait_ge(std_ready, 1)
            v_.reciprocal(small[:, 3, :], small[:, 2, :])
            dve.drain()
            v_.tensor_tensor(H[:, :, :], H[:, :, :], over(small[:, 3, :], HID), ALU.mult)
            dve.drain()
            v_.tensor_tensor(H[:, :, :], H[:, :, :], along(rows[:, ROW_G1:ROW_G1 + HID], HID), ALU.mult)
            dve.drain()
            v_.tensor_tensor(H[:, :, :], H[:, :, :], along(rows[:, ROW_BETA1:ROW_BETA1 + HID], HID), ALU.add)
            dve.drain()
            v_.tensor_scalar(H[:, :, :], H[:, :, :], 0.0, None, ALU.max)
            dve.drain().then_inc(h_ready, 1)
            with dve.Fori(1, CONVS - 1) as n:
                conv(n, HID, HID)
                v_.tensor_scalar(H[:, :, :], H[:, :, :], 0.0, None, ALU.max)
                dve.drain().then_inc(h_ready, 1)
            conv(CONVS - 1, HID, D)
            v_.tensor_add(x1[:, :, :], H[:, :, 0:D], x0[:, :, :])
            dve.drain()
            normalise(x1[:, :, :], D, 1)
            v_.tensor_copy(xn, x1[:, :, :])
            for b in range(2):
                v_.memset(msg[b][:, :, D:D + 1], 1.0)
            dve.drain().then_inc(late_free, 1)
            dve.drain().then_inc(xn_ready, 1)
            dve.wait_ge(iota_ready, 1)

            def group(layer, i, b):
                g = 2 * i + b
                q = layer * G + g
                at, vs, ve = load_visits(dve, layer, g)
                window = load_offset(dve, at, None, C - 1)
                dve.wait_ge(gates_done, q + 1)
                v_.tensor_tensor(gate.rearrange("p (a t) f -> p a t f", a=2),
                                 bank[:, 2 * b:2 * b + 2, 0:4 * D].rearrange("p a (t f) -> p a t f", f=D),
                                 b_cur.unsqueeze(1).unsqueeze(1).broadcast_to((P, 2, 4, D)), ALU.add).then_inc(gates_read, 1)
                dve.wait_ge(xg_ready[b], (layer * (G // 2) + i + 1) * (T * 16))
                dve.wait_ge(gates_read, q + 3)
                v_.tensor_tensor(msg[b][:, :, 0:D], gate, xg[b], ALU.mult).then_inc(msg_ready, 1)
                with dve.Fori(vs, ve) as v:
                    w = window(v)
                    v_.tensor_tensor(oh, dst_f[:, bass.ds(g * T, T)].unsqueeze(2).broadcast_to((P, T, P)),
                                     iota_n[:, bass.ds(w * P, P)].unsqueeze(1).broadcast_to((P, T, P)), ALU.is_equal)\
                      .then_inc(oh_ready, 1)
                    dve.wait_ge(vis_done, v + 1)
                    part = agg[:, bass.ds(w, 1), :].rearrange("p c f -> p (c f)")
                    v_.tensor_tensor(part, part, bank[:, 4, 0:D + 1], ALU.add).then_inc(agg_added, 1)
                dve.sem_inc(xg_free, 1)

            with dve.Fori(0, LAYERS) as layer:
                v_.memset(agg, 0.0)
                dve.drain()
                dve.wait_ge(w_cur_ready, (layer + 1) * 2)
                dve.wait_ge(table_written, (layer + 1) * 16)
                dve.sem_inc(sums_begun, 1)
                with dve.Fori(0, G // 2) as i:
                    for b in range(2):
                        group(layer, i, b)
                dve.drain()
                v_.tensor_scalar(small[:, 0, :], agg[:, :, D], 1.0, None, ALU.max)
                dve.drain()
                v_.reciprocal(small[:, 1, :], small[:, 0, :])
                dve.drain()
                v_.tensor_tensor(xn, agg[:, :, 0:D], over(small[:, 1, :], D), ALU.mult)
                dve.drain()
                v_.tensor_scalar(xn, xn, 0.0, None, ALU.max)
                dve.drain().then_inc(xn_ready, 1)

            v_.tensor_copy(x3, xn)
            dve.drain().then_inc(x3_ready, 1)
            for c in range(C):
                dve.wait_ge(xT_psum, c + 1)
                if c:
                    dve.wait_ge(fin_done, c)
                v_.tensor_copy(xT[0:D, :], bank[0:D, 5, 0:P]).then_inc(xT_kept, 1)
                if c:
                    v_.tensor_copy(xn[:, c - 1, :], bank[:, 6 + (c - 1) % 2, 0:D]).then_inc(fin_read, 1)
            dve.wait_ge(fin_done, C)
            v_.tensor_copy(xn[:, C - 1, :], bank[:, 6 + (C - 1) % 2, 0:D])
            dve.drain()
            v_.tensor_tensor(xn, xn, along(rows[:, ROW_BOUT:ROW_BOUT + D], D), ALU.add)
            dve.drain()
            v_.tensor_add(xn, xn, x1[:, :, :])
            dve.drain()
            normalise(xn, D, 2)
            dve.drain().then_inc(out_ready, 1)


def kernel(**inputs):
    import numpy as np
    import concourse.bacc as bacc
    from concourse import mybir as mb
    from concourse.bass_utils import run_bass_kernel_spmd

    a = {k: np.asarray(v) for k, v in inputs.items()}

    def index_layout(v):
        out = np.full((G * GROUP,), NODES_PAD - 1, v.dtype)
        out[:N_EDGES] = v
        return np.ascontiguousarray(out.reshape(G, P, T).transpose(1, 0, 2).reshape(P, G * T))

    edge = np.zeros((EDGES_PAD, D), np.float32)
    edge[:N_EDGES] = a["edge_attr_64"]
    edge = edge.reshape(G, P, 2, T // 2, D).transpose(0, 2, 4, 3, 1).reshape(G, P, (T // 2) * P)

    x = np.zeros((NODES_PAD, D), np.float32)
    x[:N_NODES] = a["x"]
    x = x.reshape(C, P, D).transpose(1, 0, 2)

    w = np.zeros((P, WEIGHTS), np.float32)
    for n in range(CONVS):
        m = a[f"L0_gnn_W{n + 1}"]
        w[:m.shape[0], W_L0 + n * HID:W_L0 + n * HID + m.shape[1]] = m
    for n in range(LAYERS):
        for half in range(2):
            w[half * D:(half + 1) * D, W_L1 + n * D:W_L1 + (n + 1) * D] = a[f"L1_gnn_W{n + 1}"].T
    w[:D, W_OUT:W_OUT + D] = a["L1_gnn_Wout"].T

    row = np.zeros((ROWS,), np.float32)
    for n in range(CONVS):
        b = a[f"L0_gnn_b{n + 1}"]
        row[ROW_B + n * HID:ROW_B + n * HID + b.shape[0]] = b
    row[ROW_G1:ROW_G1 + HID] = a["L0_gnn_g1"]
    row[ROW_BETA1:ROW_BETA1 + HID] = a["L0_gnn_beta1"]
    for n in range(LAYERS):
        row[ROW_L1B + n * D:ROW_L1B + (n + 1) * D] = a[f"L1_gnn_b{n + 1}"]
    row[ROW_BOUT:ROW_BOUT + D] = a["L1_gnn_bout"]
    rows = np.tile(row, (P, 1))

    arrays = {
        "src": index_layout(a["src"]), "dst": index_layout(a["dst"]), "edge": np.ascontiguousarray(edge),
        "x": np.ascontiguousarray(x), "w": w, "rows": rows,
    }
    nc = bacc.Bacc("TRN2", target_bir_lowering=False, num_devices=1)
    args = [nc.dram_tensor("in_" + k, v.shape, mb.dt.from_np(v.dtype), kind="ExternalInput").ap() for k, v in arrays.items()]
    out = nc.dram_tensor("out", [N_NODES, D], mb.dt.float32, kind="ExternalOutput").ap()
    gnn_program(nc, *args, out)
    r = run_bass_kernel_spmd(nc, [{"in_" + k: v for k, v in arrays.items()}], core_ids=[0])
    return r.results[0]["out"]
```
